# Optimizing a Trainium2 kernel written in Bass

```python
import numpy as np
import jax
import jax.numpy as jnp

def _softmax(x, axis=-1):
    return jax.nn.softmax(x, axis=axis)

def _gelu(x):
    return jax.nn.gelu(x, approximate=True)

def _silu(x):
    return jax.nn.silu(x)

def _sigmoid(x):
    return jax.nn.sigmoid(x)

def _layernorm(x, axis=-1, eps=1e-05):
    m = jnp.mean(x, axis=axis, keepdims=True)
    v = jnp.var(x, axis=axis, keepdims=True)
    return (x - m) / jnp.sqrt(v + eps)

def _scatter_add(tgt, idx, src, axis=0):
    return tgt.at[idx].add(src)

def _segment_sum(src, seg, n):
    return jax.ops.segment_sum(src, seg, n)
kernel_name = 'mk_seq_preln_d2_jaxref_r8_3bffae'

def setup_inputs(seed: int=0):
    np.random.seed(seed)
    _w = jnp.asarray

    def _L0_attn_setup():
        import jax, jax.numpy as jnp
        import numpy as np
        B, S, D_MODEL, D_K = (4, 256, 128, 1)
        D_QKV = D_MODEL * D_K
        MASK_NEG = -9000000000000000.0

        def _scaled_dot_product_attention(q, k, v):
            d_k = k.shape[-1]
            scores = jnp.einsum('bqd,bkd->bqk', q, k) / jnp.sqrt(jnp.float32(d_k))
            scores = jnp.triu(scores, k=0)
            scores = jnp.where(scores == 0, MASK_NEG, scores)
            attn = jax.nn.softmax(scores, axis=-1)
            return jnp.einsum('bqk,bkd->bqd', attn, v)
        key = jax.random.key(seed)
        kx, kw = jax.random.split(key)
        x = jax.random.normal(kx, (B, S, D_MODEL), dtype=jnp.float32)
        W = jax.random.normal(kw, (D_MODEL, 3 * D_QKV), dtype=jnp.float32) * (1.0 / np.sqrt(D_MODEL))
        return {'x': x, 'W': W}
    _L0_attn_in = _L0_attn_setup()

    def _L0_ffn_setup():
        import jax, jax.numpy as jnp
        import numpy as np
        B, S, H = (4, 256, 128)
        E, K = (8, 2)
        I_R, I_S = (4 * H, 8 * H)
        CAP_FACTOR = 1.25
        SCALE = 1.0
        key = jax.random.key(seed)
        ks = jax.random.split(key, 9)
        std = 0.02
        return {'x': jax.random.normal(ks[0], (B, S, H), jnp.float32), 'router_w': std * jax.random.normal(ks[1], (E, H), jnp.float32), 'rg': std * jax.random.normal(ks[2], (E, H, I_R), jnp.float32), 'ru': std * jax.random.normal(ks[3], (E, H, I_R), jnp.float32), 'rd': std * jax.random.normal(ks[4], (E, I_R, H), jnp.float32), 'sg': std * jax.random.normal(ks[5], (H, I_S), jnp.float32), 'su': std * jax.random.normal(ks[6], (H, I_S), jnp.float32), 'sd': std * jax.random.normal(ks[7], (I_S, H), jnp.float32)}
    _L0_ffn_in = _L0_ffn_setup()

    def _L1_attn_setup():
        import jax, jax.numpy as jnp
        import numpy as np
        import math
        NUM_HEADS = 16
        MAX_BIAS = 8.0

        def _alibi_slopes(n_heads):

            def slopes(n):
                start = 2.0 ** (-2 ** (-(math.log2(n) - 3)))
                return [start * start ** i for i in range(n)]
            if math.log2(n_heads).is_integer():
                s = slopes(n_heads)
            else:
                p = 2 ** math.floor(math.log2(n_heads))
                s = slopes(p) + slopes(2 * p)[0::2][:n_heads - p]
            return jnp.asarray(np.array(s, dtype=np.float32))
        key = jax.random.key(seed)
        ks = jax.random.split(key, 5)
        B, S, C = (2, 256, 128)
        return {'x': jax.random.normal(ks[0], (B, S, C), jnp.float32), 'in_proj_weight': jax.random.normal(ks[1], (3 * C, C), jnp.float32) * C ** (-0.5), 'in_proj_bias': jax.random.normal(ks[2], (3 * C,), jnp.float32) * 0.02, 'out_proj_weight': jax.random.normal(ks[3], (C, C), jnp.float32) * C ** (-0.5), 'out_proj_bias': jax.random.normal(ks[4], (C,), jnp.float32) * 0.02}
    _L1_attn_in = _L1_attn_setup()

    def _L1_ffn_setup():
        import jax, jax.numpy as jnp
        import numpy as np
        E, D, F, GATE_DIM = (8, 128, 512, 16)
        B, T = (2, 256)
        key = jax.random.key(seed)
        ks = jax.random.split(key, 7)
        s = 0.02
        return {'hidden_states': jax.random.normal(ks[0], (B, T, D), dtype=jnp.float32), 'w_red': jax.random.normal(ks[1], (D, GATE_DIM), dtype=jnp.float32) * s, 'wg': jax.random.normal(ks[2], (E, GATE_DIM), dtype=jnp.float32), 'w1': jax.random.normal(ks[3], (E, D, F), dtype=jnp.float32) * s, 'b1': jax.random.normal(ks[4], (E, F), dtype=jnp.float32) * s, 'w2': jax.random.normal(ks[5], (E, F, D), dtype=jnp.float32) * s, 'b2': jax.random.normal(ks[6], (E, D), dtype=jnp.float32) * s}
    _L1_ffn_in = _L1_ffn_setup()
    _d = {'L0_attn_x': _L0_attn_in['x'], 'L0_attn_W': _L0_attn_in['W'], 'L0_ffn_router_w': _L0_ffn_in['router_w'], 'L0_ffn_rg': _L0_ffn_in['rg'], 'L0_ffn_ru': _L0_ffn_in['ru'], 'L0_ffn_rd': _L0_ffn_in['rd'], 'L0_ffn_sg': _L0_ffn_in['sg'], 'L0_ffn_su': _L0_ffn_in['su'], 'L0_ffn_sd': _L0_ffn_in['sd'], 'L1_attn_in_proj_weight': _L1_attn_in['in_proj_weight'], 'L1_attn_in_proj_bias': _L1_attn_in['in_proj_bias'], 'L1_attn_out_proj_weight': _L1_attn_in['out_proj_weight'], 'L1_attn_out_proj_bias': _L1_attn_in['out_proj_bias'], 'L1_ffn_w_red': _L1_ffn_in['w_red'], 'L1_ffn_wg': _L1_ffn_in['wg'], 'L1_ffn_w1': _L1_ffn_in['w1'], 'L1_ffn_b1': _L1_ffn_in['b1'], 'L1_ffn_w2': _L1_ffn_in['w2'], 'L1_ffn_b2': _L1_ffn_in['b2']}
    _x0 = _d['L0_attn_x']
    _d['L0_attn_x'] = jax.random.normal(jax.random.fold_in(jax.random.key(seed), 1), (16, 256, 128), dtype=_x0.dtype)
    del _x0
    return _d

def reference(L0_attn_x, L0_attn_W, L0_ffn_router_w, L0_ffn_rg, L0_ffn_ru, L0_ffn_rd, L0_ffn_sg, L0_ffn_su, L0_ffn_sd, L1_attn_in_proj_weight, L1_attn_in_proj_bias, L1_attn_out_proj_weight, L1_attn_out_proj_bias, L1_ffn_w_red, L1_ffn_wg, L1_ffn_w1, L1_ffn_b1, L1_ffn_w2, L1_ffn_b2):

    def _L0_attn_ref(x, W):
        import jax, jax.numpy as jnp
        import numpy as np
        B, S, D_MODEL, D_K = (4, 256, 128, 1)
        D_QKV = D_MODEL * D_K
        MASK_NEG = -9000000000000000.0

        def _scaled_dot_product_attention(q, k, v):
            d_k = k.shape[-1]
            scores = jnp.einsum('bqd,bkd->bqk', q, k) / jnp.sqrt(jnp.float32(d_k))
            scores = jnp.triu(scores, k=0)
            scores = jnp.where(scores == 0, MASK_NEG, scores)
            attn = jax.nn.softmax(scores, axis=-1)
            return jnp.einsum('bqk,bkd->bqd', attn, v)
        qkv = jnp.einsum('bsd,df->bsf', x, W)
        q, k, v = jnp.split(qkv, 3, axis=-1)
        return _scaled_dot_product_attention(q, k, v)

    def _L0_ffn_ref(x, router_w, rg, ru, rd, sg, su, sd):
        import jax, jax.numpy as jnp
        import numpy as np
        B, S, H = (4, 256, 128)
        E, K = (8, 2)
        I_R, I_S = (4 * H, 8 * H)
        CAP_FACTOR = 1.25
        SCALE = 1.0
        b, s, h = x.shape
        T = b * s
        capacity = max(int(CAP_FACTOR * T / E), 1)
        xf = x.reshape(T, h)
        eps = jnp.finfo(x.dtype).eps
        xn = xf * jax.lax.rsqrt(jnp.mean(xf * xf, axis=-1, keepdims=True) + eps)
        logits = xn @ router_w.T
        probs = jax.nn.softmax(logits, axis=-1)
        topk_p, topk_i = jax.lax.top_k(probs, K)
        rw = topk_p / jnp.sum(topk_p, axis=-1, keepdims=True)
        one_hot = jax.nn.one_hot(topk_i, E, dtype=x.dtype)
        mask = one_hot.sum(1)
        wdense = (one_hot * rw[..., None]).sum(1)
        sel = mask.T.astype(bool)
        order = jnp.argsort(~sel, axis=1, stable=True)
        dispatch = order[:, :capacity]
        count = sel.sum(axis=1)
        valid = (jnp.arange(capacity)[None, :] < count[:, None]).astype(x.dtype)
        xg = xf[dispatch]
        gate = jax.nn.silu(jnp.einsum('ech,ehi->eci', xg, rg))
        up = jnp.einsum('ech,ehi->eci', xg, ru)
        eout = jnp.einsum('eci,eih->ech', gate * up, rd)
        w = jnp.take_along_axis(wdense.T, dispatch, axis=1)
        contrib = eout * (w * valid)[..., None]
        routed = jnp.zeros_like(xf).at[dispatch.reshape(-1)].add(contrib.reshape(-1, h))
        shared = jax.nn.silu(x @ sg) * (x @ su) @ sd
        return shared + SCALE * routed.reshape(b, s, h)

    def _L1_attn_ref(x, in_proj_weight, in_proj_bias, out_proj_weight, out_proj_bias):
        import jax, jax.numpy as jnp
        import numpy as np
        import math
        NUM_HEADS = 16
        MAX_BIAS = 8.0

        def _alibi_slopes(n_heads):

            def slopes(n):
                start = 2.0 ** (-2 ** (-(math.log2(n) - 3)))
                return [start * start ** i for i in range(n)]
            if math.log2(n_heads).is_integer():
                s = slopes(n_heads)
            else:
                p = 2 ** math.floor(math.log2(n_heads))
                s = slopes(p) + slopes(2 * p)[0::2][:n_heads - p]
            return jnp.asarray(np.array(s, dtype=np.float32))
        B, S, C = x.shape
        H = NUM_HEADS
        D = C // H
        qkv = x @ in_proj_weight.T + in_proj_bias
        qkv = qkv.reshape(B, S, 3, H, D).transpose(2, 0, 3, 1, 4)
        q, k, v = (qkv[0], qkv[1], qkv[2])
        slopes = _alibi_slopes(H)
        pos = jnp.arange(S, dtype=jnp.float32)
        rel = pos[:, None] - pos[None, :]
        bias = jnp.minimum(rel[None, :, :] * slopes[:, None, None], MAX_BIAS)
        scores = jnp.einsum('bhqd,bhkd->bhqk', q, k) * D ** (-0.5) + bias[None]
        probs = jax.nn.softmax(scores, axis=-1)
        out = jnp.einsum('bhqk,bhkd->bhqd', probs, v)
        out = out.transpose(0, 2, 1, 3).reshape(B, S, C)
        return out @ out_proj_weight.T + out_proj_bias

    def _L1_ffn_ref(hidden_states, w_red, wg, w1, b1, w2, b2):
        import jax, jax.numpy as jnp
        import numpy as np
        E, D, F, GATE_DIM = (8, 128, 512, 16)
        B, T = (2, 256)
        b, t, c = hidden_states.shape
        x = hidden_states.reshape(-1, c)
        red = x @ w_red
        wg_n = wg / jnp.maximum(jnp.linalg.norm(wg, axis=1, keepdims=True), 0.0001)
        logits = red @ wg_n.T
        gates = jax.nn.softmax(logits, axis=1)
        idx = jnp.argmax(gates, axis=1)
        scores = jnp.take_along_axis(gates, idx[:, None], axis=1)
        h = jax.nn.gelu(jnp.einsum('td,edf->etf', x, w1) + b1[:, None, :], approximate=False)
        y = jnp.einsum('etf,efd->etd', h, w2) + b2[:, None, :]
        out = jnp.take_along_axis(y, idx[None, :, None], axis=0)[0]
        out = out * scores
        return out.reshape(b, t, c)
    x = L0_attn_x
    x = x + _L0_attn_ref(_layernorm(x, axis=-1), L0_attn_W)
    x = x + _L0_ffn_ref(_layernorm(x, axis=-1), L0_ffn_router_w, L0_ffn_rg, L0_ffn_ru, L0_ffn_rd, L0_ffn_sg, L0_ffn_su, L0_ffn_sd)
    x = x + _L1_attn_ref(_layernorm(x, axis=-1), L1_attn_in_proj_weight, L1_attn_in_proj_bias, L1_attn_out_proj_weight, L1_attn_out_proj_bias)
    x = x + _L1_ffn_ref(_layernorm(x, axis=-1), L1_ffn_w_red, L1_ffn_wg, L1_ffn_w1, L1_ffn_b1, L1_ffn_w2, L1_ffn_b2)
    return x

_drawn_inputs = setup_inputs


def setup_inputs(seed=0):
    import zlib

    import numpy as np

    out = dict(_drawn_inputs(seed))
    spreads = {}
    factors = {'L0_ffn_router_w': 8.0,
     'L0_ffn_rg': 8.0,
     'L0_ffn_ru': 8.0,
     'L0_ffn_rd': 8.0,
     'L0_ffn_sg': 3.364,
     'L0_ffn_su': 3.342,
     'L0_ffn_sd': 3.333,
     'L1_attn_out_proj_bias': 2.918,
     'L1_ffn_w_red': 6.55,
     'L1_ffn_wg': 6.534,
     'L1_ffn_w1': 6.676,
     'L1_ffn_b1': 8.0,
     'L1_ffn_w2': 6.547,
     'L1_ffn_b2': 29.193,
     'L1_attn_in_proj_bias': 2.814}
    for name, (base, spread) in spreads.items():
        noise = np.random.default_rng([zlib.crc32(name.encode()), seed]).standard_normal(out[name].shape)
        drawn = base * np.exp(spread * noise) if base else spread * noise
        out[name] = jnp.asarray(drawn.astype(out[name].dtype))
    for name, factor in factors.items():
        out[name] = (out[name] * factor).astype(out[name].dtype)
    return out
```

```python
from contextlib import ExitStack

import numpy as np

import concourse.bass as bass
import concourse.mybir as mybir

F32 = mybir.dt.float32
BF16 = mybir.dt.bfloat16
I32 = mybir.dt.int32
U32 = mybir.dt.uint32
ALU = mybir.AluOpType
ACT = mybir.ActivationFunctionType
AX = mybir.AxisListType.X

P = 128
BATCH, SEQ, D = 16, 256, 128
T = BATCH * SEQ
NT = T // P
QT = SEQ // P
LN_EPS = 1e-5
NEG = -9e15

E0, I0, IS0 = 8, 512, 1024
CAP = 5 * T // 4 // E0
CT = CAP // P
SLOTS = E0 * CAP
HALF = CAP // 2
RMS_EPS = float(np.finfo(np.float32).eps)
GT = 4
NG = NT // GT
BIG = 3e38
NH, HD = 16, 8
SLOPES = [float(np.float32(2.0 ** (-0.5 * (i + 1)))) for i in range(NH)]
MAX_BIAS = 8.0
PARTS = 3
TILE = 32
HG = P // TILE
KROWS = PARTS * PARTS * HD
QK_SCALE = float(HD) ** -0.5
E1, I1, GD = 8, 512, 16
TILES = NT + E1
ROW = D + 4
NO_TOKEN = 1 << 20
W_ALL = 2 * I1 + I1 // P + D
DVE_COPIES = (1, 3, 7, 9, 11, 15)

STAGE = 4


def alive(b, n):
    return not isinstance(b, int) or 0 <= b < n


def pipelined(eng, step, n, lag, peel=2, places=2, ahead=0):
    for b in range(peel):
        step(b, b % places)
    with eng.Fori(peel // places, (n - ahead) // places) as i:
        for k in range(places):
            step(places * i + k, k)
    for b in range(n - ahead, n + lag):
        step(b, b % places)


def build(nc, t):
    ctx = ExitStack()
    with ctx:
        _build(nc, t, ctx)


def _build(nc, t, ctx):
    def sb(name, shape, dt=F32):
        return ctx.enter_context(nc.sbuf_tensor(name, shape, dt))

    def sem(name):
        return ctx.enter_context(nc.semaphore(name))

    bank = [ctx.enter_context(nc.psum_tensor(f"bank{n}", [P, 512], F32)) for n in range(8)]

    x = sb("x", [P, NT, D])
    ident = sb("ident", [P, P])
    stats = sb("stats", [P, NT, 6])
    mean = sb("mean", [P, NT])
    var = sb("var", [P, NT])
    rstd = sb("rstd", [P, NT])
    ln_tmp = sb("ln_tmp", [P, 4, NT])
    token_no = sb("token_no", [P, NT])
    minus_half = sb("minus_half", [P, NT])

    slot = sb("slot", [P, NT, 2], U32)
    slot_back = sb("slot_back", [P, NT, 2], U32)
    gate_w = sb("gate_w", [P, NT, 2])
    zeros = sb("zeros", [P, P])
    upper = sb("upper", [P, P], BF16)
    ones_b = sb("ones_b", [P, P], BF16)
    iota_e = sb("iota_e", [P, NT, E0])
    spare_slot = sb("spare_slot", [P, NT, 2])
    ones_t = sb("ones_t", [P, NT])

    rt = [sb(f"rt{k}", [P, NT, E0])[:] for k in range(6)]
    rs = [sb(f"rs{k}", [P, NT])[:] for k in range(8)]
    tile_rs = sb("tile_rs", [P, 3, E1])
    owner = sb("owner", [P, TILES])[:]
    oh = sb("oh", [P, 2, NT, E0])[:]
    picked_b = sb("picked_b", [P, NT, E0], BF16)[:]

    alibi = sb("alibi", [P, NH, SEQ + P])
    w3 = sb("w3", [P, 3 * D])
    w_out = sb("w_out", [P, D])
    bqk = sb("bqk", [P, 2])
    bv = sb("bv", [P, D])
    bo = sb("bo", [P, D])
    w_redT = sb("w_redT", [GD, D])
    wgT = sb("wgT", [GD, E1])
    wg_all = sb("wg_all", [P, E1, GD])
    w_gate = sb("w_gate", [P, E1])
    inv_norm = sb("inv_norm", [P, E1])
    half = sb("half", [P, E1])
    tile_no = sb("tile_no", [P, TILES, E1])
    empty_row = sb("empty_row", [P, ROW])
    send5_slot = sb("send5_slot", [P, 4, 1], U32)
    slot5 = sb("slot5", [P, NT], U32)
    n_int = sb("n_int", [P, E1], I32)
    tile_expert = sb("tile_expert", [P, TILES], I32)
    token = sb("token", [P, 2, 1], U32)
    give_slot = sb("give_slot", [P, 2, 2 * QT], U32)

    ARENA = 34 * 1024
    arena = sb("arena", [P, ARENA])
    used = [0]

    def carve(shape, dt=F32):
        n = int(np.prod(shape[1:])) * (2 if dt == BF16 else 4) // 4
        a = arena[:, used[0]:used[0] + n]
        used[0] += n
        assert used[0] <= ARENA, used
        if dt != F32:
            a = a.bitcast(dt)
        if len(shape) > 2:
            names = "abcde"[:len(shape) - 1]
            a = a.rearrange(f"p ({' '.join(names)}) -> p {' '.join(names)}",
                            **{n: m for n, m in zip(names[1:], shape[2:])})
        return a

    hidden = carve([P, 2, IS0 // P, GT * P])
    after_hidden, used[0] = used[0], 0

    wqkv = carve([P, 3 * D])
    keep = carve([P, QT, SEQ])
    h = carve([P, 2, QT, D])
    hT = carve([P, 2, SEQ])
    qk = carve([P, 2, 2, SEQ])
    v = carve([P, 2, QT, D])
    scores = carve([P, 2, QT, SEQ])
    zeros_masked = carve([P, QT, SEQ])
    negmax = carve([P, 2, QT])
    rowmax = carve([P, 2, QT])
    probs = carve([P, 2, QT, SEQ])
    rowsum = carve([P, 2, QT])
    rinv = carve([P, 2, QT])
    probsT = carve([P, QT, SEQ])

    used[0] = max(used[0], after_hidden)
    xf = carve([P, NT, D])
    xfT = carve([P, T])
    h4 = carve([P, 2, GT, D])
    xf_tile = carve([P, 2, GT * P])
    w_router = carve([P, E0])
    w_sg = carve([P, IS0])
    w_su = carve([P, IS0])
    w_sd = carve([P, IS0 // P, D])
    sil = carve([P, 2, GT * P])
    w_eg = carve([P, 2, I0])
    w_eu = carve([P, 2, I0])
    w_ed = carve([P, 2, I0 // P, D])
    xg = carve([P, 2, CT, D])
    xgT = carve([P, 2, CAP])
    eo = carve([P, 2, CT, D])
    r_rms = carve([P, NT])
    rk = [carve([P, NT, 2]) for _ in range(5)]
    send_rows = carve([P, 4, D])
    send_slot = sb("send_slot", [P, 4, 2], U32)

    used[0] = 0
    qs = carve([P, 2, NH, SEQ], BF16)
    ks = carve([P, 2, NH, SEQ], BF16)
    given = carve([P, 2, 2 * QT, D])
    bn3 = carve([P, 2, QT, 6])
    mv = carve([P, 2, QT, 3])
    rstd3 = carve([P, 2, QT])
    h3 = carve([P, 2, QT, D])
    hT3 = carve([P, SEQ])
    qkf = carve([P, 2, SEQ])
    qkr = carve([P, 2, SEQ])
    part = carve([P, 2, PARTS, SEQ], BF16)
    v3 = carve([P, 2, QT, NH, TILE])
    sc3 = carve([P, 4, QT, SEQ])
    nmax3 = carve([P, 4, QT])
    pr3 = carve([P, 4, QT, SEQ])
    prT3 = carve([P, 2 * HG, QT, SEQ])
    oTu = carve([P, NH // HG, SEQ])
    rinv3 = carve([P, QT, NH])
    o3 = carve([P, QT, D])
    oT3 = carve([P, SEQ])

    w_all = carve([P, E1, W_ALL])
    used[0] = 0
    h5 = carve([P, 2, GT, D])
    h5T = carve([P, 2, GT * P])
    w_own = carve([P, 4, W_ALL])
    extra = carve([P, NT, 4])
    send5 = carve([P, 4, ROW])
    xr = carve([P, 4, ROW])
    hj = carve([P, 2, D])
    hjT = carve([P, 2, P])
    gj = carve([P, 2, I1 // P, P])
    yj = carve([P, 2, D])
    rj = carve([P, 2, D])

    XC = 4
    x_in = [sem(f"x_in{c}") for c in range(XC)]
    w_in = sem("w_in")
    const_zero = sem("const_zero")
    const_done = sem("const_done")
    stats_done = sem("stats_done")
    var_done = sem("var_done")
    rstd_done = sem("rstd_done")
    dve_chain = sem("dve_chain")
    ln_done = sem("ln_done")
    tr_done = sem("tr_done")
    hT_done = sem("hT_done")
    qk_mm = sem("qk_mm")
    v_mm = sem("v_mm")
    qk_done = sem("qk_done")
    v_done = sem("v_done")
    s_mm = sem("s_mm")
    s_read = sem("s_read")
    mask_a = sem("mask_a")
    mask_b = sem("mask_b")
    mask_done = sem("mask_done")
    max_done = sem("max_done")
    exp_done = sem("exp_done")
    pT_tr = sem("pT_tr")
    pT_done = sem("pT_done")
    pv_mm = sem("pv_mm")
    rinv_done = sem("rinv_done")
    att_done = sem("att_done")
    out_done = sem("out_done")
    zeros_set = sem("zeros_set")
    prefill = sem("prefill")
    ms_done = sem("ms_done")
    rms_done = sem("rms_done")
    h4_done = sem("h4_done")
    xf_done = sem("xf_done")
    tr4_done = sem("tr4_done")
    xfT_done = sem("xfT_done")
    xft_done = sem("xft_done")
    router_mm = sem("router_mm")
    d12_done = sem("d12_done")
    e2_done = sem("e2_done")
    picked = sem("picked")
    count_mm = sem("count_mm")
    slots_done = sem("slots_done")
    w_router_in = sem("w_router_in")
    w_shared_in = sem("w_shared_in")
    staged = sem("staged")
    sent = [sem(f"sent{k}") for k in range(4)]
    gu_mm = sem("gu_mm")
    sil_done = sem("sil_done")
    hid_done = sem("hid_done")
    down_mm = sem("down_mm")
    down_read = sem("down_read")
    ew_in = [sem(f"ew_in{k}") for k in range(2)]
    xg_in = [sem(f"xg_in{k}") for k in range(2)]
    xg_tr = sem("xg_tr")
    xgT_done = sem("xgT_done")
    eo_out = [sem(f"eo_out{k}") for k in range(2)]

    x_dram = t["L0_attn_x"].rearrange("b (u p) d -> p (b u) d", p=P)
    out_dram = t["out"].rearrange("b (u p) d -> p (b u) d", p=P)

    w3_in = sem("w3_in")
    waits_met = sem("waits_met")
    alibi_done = sem("alibi_done")
    give_staged = sem("give_staged")
    given_in = [sem(f"given_in{k}") for k in range(2)]
    comb_a = sem("comb_a")
    comb_done = sem("comb_done")
    st_a = sem("st_a")
    st_b = sem("st_b")
    var3_done = sem("var3_done")
    rstd3_done = sem("rstd3_done")
    h3_done = sem("h3_done")
    tr3 = sem("tr3")
    hT3_done = sem("hT3_done")
    qk3_mm = sem("qk3_mm")
    v3_mm = sem("v3_mm")
    qk3_done = sem("qk3_done")
    v3_done = sem("v3_done")
    split = sem("split")
    parts_done = sem("parts_done")
    parts_out = [sem(f"parts_out{k}") for k in range(2)]
    qk3_in = [sem(f"qk3_in{k}") for k in range(2)]
    s3_mm = sem("s3_mm")
    max3_done = sem("max3_done")
    exp3_done = sem("exp3_done")
    pT3_tr = sem("pT3_tr")
    copied_d = sem("copied_d")
    copied_a = sem("copied_a")
    pv3_mm = sem("pv3_mm")
    po_copied = sem("po_copied")
    ob_tr = sem("ob_tr")
    rinv3_done = sem("rinv3_done")
    o3_done = sem("o3_done")
    oT3_tr = sem("oT3_tr")
    oT3_done = sem("oT3_done")
    out3_mm = sem("out3_mm")
    res3_a = sem("res3_a")
    res3_done = sem("res3_done")

    gate_in = sem("gate_in")
    w_all_in = sem("w_all_in")
    empty_set = sem("empty_set")
    prefill5 = sem("prefill5")
    sq_done = sem("sq_done")
    norm_root = sem("norm_root")
    gate_mm = sem("gate_mm")
    gate_done = sem("gate_done")
    h5_done = sem("h5_done")
    tr5 = sem("tr5")
    h5T_done = sem("h5T_done")
    router5_mm = sem("router5_mm")
    less_done = sem("less_done")
    exp5_done = sem("exp5_done")
    picked5 = sem("picked5")
    count5_mm = sem("count5_mm")
    slots5_done = sem("slots5_done")
    staged5 = sem("staged5")
    sent5 = [sem(f"sent5{k}") for k in range(4)]
    xr_in = [sem(f"xr_in{k}") for k in range(4)]
    hj_done = sem("hj_done")
    own_done = sem("own_done")
    trj = sem("trj")
    hjT_done = sem("hjT_done")
    up_mm = sem("up_mm")
    gelu_done = sem("gelu_done")
    down5_mm = sem("down5_mm")
    y_done = sem("y_done")
    rj_done = sem("rj_done")
    stored = [sem(f"stored{k}") for k in range(2)]

    xg_dram = nc.dram_tensor("xg_rows", (SLOTS + 2 * T, D), F32).ap()
    eo_dram = nc.dram_tensor("eo_rows", (SLOTS + 1, D), F32).ap()

    sorted_dram = nc.dram_tensor("sorted_rows", (TILES * P, ROW), F32).ap()
    out_rows = t["out"].rearrange("b s d -> (b s) d")
    part_dram = nc.dram_tensor("qk_parts", (2, 2, PARTS, P, SEQ), BF16).ap()

    def wait_apart(eng, *waits):
        for s, v in waits:
            eng.wait_ge(s, v)
            eng.sem_inc(waits_met, 1)

    def copier(c, h):
        own = h in DVE_COPIES
        n = len([k for k in range(h + 1) if (k in DVE_COPIES) == own])
        per = len(DVE_COPIES) if own else NH - len(DVE_COPIES)
        return (copied_d if own else copied_a), per * c + n

    def place_used(eng, c, h):
        group = NH // HG * c + h // HG
        if not isinstance(group, int) or group >= 2:
            eng.wait_ge(pv3_mm, group - 1)

    def keep_group(dve, c, g):
        n = NH // HG * c + g
        dve.wait_ge(pv3_mm, n + 1)
        if alive(c - 1, BATCH) and g == 0:
            dve.wait_ge(ob_tr, QT * c)
        nc.vector.tensor_copy(oTu[:, g, :], bank[4][:, 0:SEQ]).then_inc(po_copied, 1)

    def parts_n(b, p):
        return 8 * (b - p) + 16

    def item(b, p, h, lag):
        c, q = (b - 1, 1 - p) if h >= lag else (b - 2, p)
        h = (h - lag) % NH
        return c, q, h, NH * c + h

    block = ctx.enter_context(nc.Block())

    def psum_T(p):
        return bank[0][:, 256 * p:256 * p + 256]

    def psum_V(p):
        return bank[2][:, 256 * p:256 * p + 256]

    @block.sync
    def _(sp):
        for c in range(XC):
            n = NT // XC
            sp.dma_start(x[:, n * c:n * c + n, :], x_dram[:, n * c:n * c + n, :]).then_inc(x_in[c], 16)
        sp.dma_start(wqkv[:], t["L0_attn_W"]).then_inc(w_in, 16)
        for dst, src in ((w3[:], t["w3"]), (w_out[:], t["w_out"]), (bqk[:], t["bqk"]),
                         (bv[:], t["bv"].partition_broadcast(P)), (bo[:], t["bo"].partition_broadcast(P))):
            sp.dma_start(dst, src).then_inc(w3_in, 16)
        sp.dma_start(w_router, t["L0_ffn_router_w"]).then_inc(w_router_in, 16)
        sp.dma_start(w_sg, t["L0_ffn_sg"]).then_inc(w_shared_in, 16)
        sp.dma_start(w_su, t["L0_ffn_su"]).then_inc(w_shared_in, 16)
        sp.dma_start(w_sd, t["L0_ffn_sd"].rearrange("(c p) d -> p c d", p=P)).then_inc(w_shared_in, 16)
        for dst, src in ((w_redT[:], t["w_redT"]), (wgT[:], t["wgT"]), (wg_all[:], t["wg"].partition_broadcast(P))):
            sp.dma_start(dst, src).then_inc(gate_in, 16)
        sp.wait_ge(empty_set, 2)
        sp.dma_start(sorted_dram.rearrange("(p n) d -> p n d", p=P),
                     empty_row[:].unsqueeze(1).to_broadcast([P, TILES, ROW])).then_inc(prefill5, 16)
        sp.wait_ge(zeros_set, 1)
        sp.dma_start(xg_dram[0:SLOTS].rearrange("(p n) d -> p n d", p=P),
                     zeros[:].unsqueeze(1).to_broadcast([P, SLOTS // P, D])).then_inc(prefill, 16)
        sp.dma_start(eo_dram[SLOTS:SLOTS + 1], zeros[0:1, :]).then_inc(prefill, 16)

        def load_weights(e, p):
            if alive(e - 2, E0):
                sp.wait_ge(down_mm, NG + e - 1)
            sp.dma_start(w_eg[:, p], t["L0_ffn_rg"][bass.ds(e, 1)].rearrange("a d f -> d (a f)")).then_inc(ew_in[p], 16)
            sp.dma_start(w_eu[:, p], t["L0_ffn_ru"][bass.ds(e, 1)].rearrange("a d f -> d (a f)")).then_inc(ew_in[p], 16)
            sp.dma_start(w_ed[:, p], t["L0_ffn_rd"][bass.ds(e, 1)].rearrange("a (c f) d -> f (a c) d", f=P)).then_inc(ew_in[p], 16)

        def load_expert(e, p):
            if alive(e, E0):
                if alive(e - 2, E0):
                    sp.wait_ge(xg_tr, e - 1)
                sp.dma_start(xg[:, p], xg_dram[bass.ds(CAP * e, CAP)].rearrange("(j p) d -> p j d", p=P)).then_inc(xg_in[p], 16)
                if not isinstance(e, int) or e >= 2:
                    load_weights(e, p)
            c, q = e - 3, 1 - p
            if alive(c, E0):
                sp.wait_ge(down_read, NG + c + 1)
                sp.dma_start(eo_dram[bass.ds(CAP * c, CAP)].rearrange("(j p) d -> p j d", p=P), eo[:, q]).then_inc(eo_out[q], 16)

        if STAGE >= 2:
            load_weights(0, 0)
            load_weights(1, 1)
            for k in range(4):
                sp.wait_ge(sent[k], 32 * NT // 4)
            pipelined(sp, load_expert, E0, 3, 4)
        def replicate(b, p):
            wait_apart(sp, (parts_done, b + 1), *([(qk3_in[p], 96 * (b - p))] if alive(b - 2, BATCH) else []))
            sp.dma_start(part_dram[p].rearrange("w a p t -> p (w a) t"), part.rearrange("p w a t -> p (w a) t")).then_inc(parts_out[p], 16)
            wait_apart(sp, (parts_out[p], 8 * (b - p) + 16), *([(s3_mm, NH * (b - 1))] if alive(b - 2, BATCH) else []))
            rows = part_dram[p].rearrange("w a (d h) t -> w (a d) h t", d=HD)
            for a in range(PARTS):
                r = PARTS * HD * a
                sp.dma_start(ks[r:r + PARTS * HD, p], rows[1]).then_inc(qk3_in[p], 16)
                for c in range(PARTS):
                    sp.dma_start(qs[r + HD * c:r + HD * c + HD, p], rows[0, HD * a:HD * a + HD]).then_inc(qk3_in[p], 16)

        if STAGE >= 2:
            for k in range(2):
                sp.wait_ge(eo_out[k], 16 * E0 // 2)
            for n, (name, width) in enumerate((("w1", I1), ("w2", I1), ("b1", I1 // P))):
                at = (0, I1, 2 * I1)[n]
                sp.dma_start(w_all[:, :, at:at + width], t[name]).then_inc(w_all_in, 16)
            sp.dma_start(w_all[:, :, 2 * I1 + I1 // P:W_ALL], t["b2"].partition_broadcast(P)).then_inc(w_all_in, 16)
            pipelined(sp, replicate, BATCH, 0)
        def sorted_rows(j, p):
            if alive(j - 4, TILES):
                sp.wait_ge(rj_done, j - 3)
            sp.dma_start(xr[:, p], sorted_dram[bass.ds(P * j, P)]).then_inc(xr_in[p], 16)

        if STAGE == 4:
            for k in range(4):
                sp.wait_ge(sent5[k], 16 * NT // 4)
            pipelined(sp, sorted_rows, TILES, 0, 4, 4)
            for k in range(2):
                sp.wait_ge(stored[k], 16 * TILES // 2)
        if STAGE in (2, 3):
            sp.wait_ge(res3_done if STAGE == 3 else comb_done, BATCH)
            sp.dma_start(out_dram, x[:]).then_inc(out_done, 16)
            sp.wait_ge(out_done, 16)
        if STAGE == 1:
            sp.wait_ge(att_done, QT * BATCH)
            sp.dma_start(out_dram, x[:]).then_inc(out_done, 16)
            sp.wait_ge(out_done, 16)

    @block.gpsimd
    def _(pool):
        nc.gpsimd.memset(ident[:], 0.0).then_inc(const_zero, 1)
        nc.gpsimd.memset(keep[:], 1.0).then_inc(const_zero, 1)
        nc.gpsimd.memset(minus_half[:], -0.5).then_inc(const_zero, 1)
        pool.wait_ge(const_zero, 3)
        nc.gpsimd.affine_select(out=ident[:], in_=ident[:], compare_op=ALU.not_equal, fill=1.0, base=0,
                                pattern=[[-1, P]], channel_multiplier=1).then_inc(const_done, 1)
        nc.gpsimd.affine_select(out=keep[:], in_=keep[:], compare_op=ALU.is_ge, fill=0.0, base=0,
                                pattern=[[-P, QT], [1, SEQ]], channel_multiplier=-1).then_inc(const_done, 1)

        def rsqrt(n):
            pool.wait_ge(var_done, n + 1)
            nc.gpsimd.tensor_tensor(rstd[:], var[:], minus_half[:], ALU.pow).then_inc(rstd_done, 1)

        nc.gpsimd.memset(zeros[:], 0.0).then_inc(zeros_set, 1)
        nc.gpsimd.memset(ones_b[:], 1.0).then_inc(const_zero, 1)
        nc.gpsimd.memset(ones_t[:], 1.0)
        pool.wait_ge(const_zero, 4)
        nc.gpsimd.affine_select(out=upper[:], in_=ones_b[:], compare_op=ALU.is_gt, fill=0.0, base=0,
                                pattern=[[1, P]], channel_multiplier=-1)
        nc.gpsimd.iota(iota_e[:], pattern=[[0, NT], [1, E0]], base=0, channel_multiplier=0,
                       allow_small_or_imprecise_dtypes=True)
        nc.gpsimd.iota(spare_slot[:], pattern=[[2 * P, NT], [1, 2]], base=SLOTS, channel_multiplier=2,
                       allow_small_or_imprecise_dtypes=True).then_inc(const_done, 1)

        nc.gpsimd.memset(empty_row[:], 0.0).then_inc(empty_set, 1)
        pool.wait_ge(empty_set, 1)
        nc.gpsimd.memset(empty_row[:, D:D + 1], float(NO_TOKEN)).then_inc(empty_set, 1)
        nc.gpsimd.memset(half[:], 0.5)
        nc.gpsimd.iota(tile_no[:], pattern=[[1, TILES], [0, E1]], base=0, channel_multiplier=0,
                       allow_small_or_imprecise_dtypes=True)
        nc.gpsimd.iota(token_no[:], pattern=[[P, NT]], base=0, channel_multiplier=1,
                       allow_small_or_imprecise_dtypes=True).then_inc(const_done, 1)
        rsqrt(0)
        nc.gpsimd.iota(alibi[:, 0, :], pattern=[[-1, SEQ + P]], base=P, channel_multiplier=1,
                       allow_small_or_imprecise_dtypes=True).then_inc(alibi_done, 1)
        rsqrt(1)
        pool.wait_ge(ms_done, 1)
        nc.gpsimd.tensor_tensor(r_rms, r_rms, minus_half[:], ALU.pow).then_inc(rms_done, 1)

        def keep_rows(g, p):
            wait_apart(pool, (h4_done, g + 1))
            nc.gpsimd.tensor_copy(xf[:, bass.ds(GT * g, GT), :], h4[:, p]).then_inc(xf_done, 1)

        pipelined(pool, keep_rows, NG, 0)

        def send(i):
            for k in range(4):
                if not isinstance(i, int):
                    pool.wait_ge(sent[k], 32 * i)
                nc.gpsimd.tensor_copy(send_rows[:, k, :], xf[:, 4 * i + k, :])
                nc.gpsimd.tensor_copy(send_slot[:, k, :], slot[:, 4 * i + k, :]).then_inc(staged, 1)
            wait_apart(pool, (staged, 4 * i + 4))
            for k in range(4):
                for j in range(2):
                    nc.gpsimd.indirect_dma_start(out=xg_dram, out_offset=bass.IndirectOffsetOnAxis(ap=send_slot[:, k, j:j + 1], axis=0),
                                                 in_=send_rows[:, k, :], in_offset=None).then_inc(sent[k], 16)

        pool.wait_ge(slots_done, 1)
        pool.wait_ge(prefill, 32)
        send(0)
        with pool.Fori(1, NT // 4) as i:
            send(i)

        def give(b, p):
            if alive(b - 2, BATCH):
                wait_apart(pool, (comb_done, b - 1))
            for u in range(QT):
                nc.gpsimd.tensor_copy(give_slot[:, p, 2 * u:2 * u + 2], slot_back[:, 2 * b + u, :]).then_inc(give_staged, 1)
            wait_apart(pool, (give_staged, 2 * b + 2))
            for j in range(2 * QT):
                nc.gpsimd.indirect_dma_start(out=given[:, p, j, :], out_offset=None, in_=eo_dram,
                                             in_offset=bass.IndirectOffsetOnAxis(ap=give_slot[:, p, j:j + 1], axis=0)).then_inc(given_in[p], 16)

        def root(b, p):
            pool.wait_ge(var3_done, b + 1)
            nc.gpsimd.tensor_tensor(rstd3[:, p], mv[:, p, :, 2], minus_half[:, 0:QT], ALU.pow).then_inc(rstd3_done, 1)

        def prepare(b, p):
            if alive(b + 1, BATCH):
                give(b + 1, 1 - p)
            wait_apart(pool, (qk3_done, b + 1), *([(parts_out[1 - p], parts_n(b - 1, 1 - p))] if alive(b - 1, BATCH) else []))
            nc.gpsimd.tensor_copy(part[:, :, 0, :], qkf).then_inc(split, 1)
            wait_apart(pool, (split, 3 * b + 1))
            nc.gpsimd.tensor_tensor(qkr, qkf, part[:, :, 0, :], ALU.subtract).then_inc(split, 1)
            wait_apart(pool, (split, 3 * b + 2))
            nc.gpsimd.tensor_copy(part[:, :, 1, :], qkr).then_inc(split, 1)
            wait_apart(pool, (split, 3 * b + 3))
            nc.gpsimd.tensor_tensor(part[:, :, 2, :], qkr, part[:, :, 1, :], ALU.subtract).then_inc(parts_done, 1)
            if alive(b + 1, BATCH):
                root(b + 1, 1 - p)

        for k in range(2):
            pool.wait_ge(eo_out[k], 16 * E0 // 2)
        give(0, 0)
        root(0, 0)
        pipelined(pool, prepare, BATCH, 0, ahead=2)

        rsqrt(2)
        pool.wait_ge(sq_done, 1)
        nc.gpsimd.tensor_tensor(inv_norm[:], inv_norm[:], half[:], ALU.pow).then_inc(norm_root, 1)

        def send_sorted(i):
            for k in range(4):
                if not isinstance(i, int):
                    pool.wait_ge(sent5[k], 16 * i)
                nc.gpsimd.tensor_copy(send5[:, k, 0:D], x[:, 4 * i + k, :])
                nc.gpsimd.tensor_copy(send5[:, k, D:ROW], extra[:, 4 * i + k, :])
                nc.gpsimd.tensor_copy(send5_slot[:, k, :], slot5[:, bass.ds(4 * i + k, 1)]).then_inc(staged5, 1)
            wait_apart(pool, (staged5, 4 * i + 4))
            for k in range(4):
                nc.gpsimd.indirect_dma_start(out=sorted_dram, out_offset=bass.IndirectOffsetOnAxis(ap=send5_slot[:, k, :], axis=0),
                                             in_=send5[:, k, :], in_offset=None).then_inc(sent5[k], 16)

        def store(j, p):
            wait_apart(pool, (rj_done, j + 1))
            nc.gpsimd.indirect_dma_start(out=out_rows, out_offset=bass.IndirectOffsetOnAxis(ap=token[:, p, :], axis=0),
                                         in_=rj[:, p, :], in_offset=None, bounds_check=T - 1,
                                         oob_is_err=False).then_inc(stored[p], 16)

        if STAGE == 4:
            pool.wait_ge(slots5_done, 1)
            pool.wait_ge(prefill5, 16)
            send_sorted(0)
            with pool.Fori(1, NT // 4) as i:
                send_sorted(i)
            pipelined(pool, store, TILES, 0)

    chain = [0]

    def hidden_e(p):
        return hidden[:, p].rearrange("p c t -> p (c t)")[:, 0:I0 // P * CAP].rearrange("p (c t) -> p c t", t=CAP)

    def eo_count(e, p):
        return 8 * (e - p)

    @block.vector
    def _(dve):
        def link(ins):
            chain[0] += 1
            ins.then_inc(dve_chain, 1)
            dve.wait_ge(dve_chain, chain[0])

        def norm_stats():
            m0, m1 = stats[:, :, 1], stats[:, :, 4]
            v0, v1 = stats[:, :, 2], stats[:, :, 5]
            link(nc.vector.tensor_tensor(ln_tmp[:, 0, :], m0, m1, ALU.add))
            nc.vector.tensor_scalar(mean[:], ln_tmp[:, 0, :], 0.5, None, ALU.mult)
            link(nc.vector.tensor_tensor(ln_tmp[:, 1, :], m0, m1, ALU.subtract))
            link(nc.vector.tensor_tensor(ln_tmp[:, 2, :], ln_tmp[:, 1, :], ln_tmp[:, 1, :], ALU.mult))
            nc.vector.tensor_tensor(ln_tmp[:, 3, :], v0, v1, ALU.add)
            link(nc.vector.tensor_scalar(ln_tmp[:, 2, :], ln_tmp[:, 2, :], D / 4.0, None, ALU.mult))
            link(nc.vector.tensor_tensor(ln_tmp[:, 3, :], ln_tmp[:, 2, :], ln_tmp[:, 3, :], ALU.add))
            nc.vector.tensor_scalar(var[:], ln_tmp[:, 3, :], 1.0 / D, LN_EPS, ALU.mult,
                                    ALU.add).then_inc(var_done, 1)

        for c in range(XC):
            n = NT // XC
            dve.wait_ge(x_in[c], 16)
            with dve.Fori(n // 4 * c, n // 4 * (c + 1)) as i:
                for u in range(4):
                    last = nc.vector.bn_stats(stats[:, 4 * i + u, :], x[:, 4 * i + u, :])
                last.then_inc(stats_done, 1)
        dve.wait_ge(stats_done, NT // 4)
        norm_stats()
        dve.wait_ge(rstd_done, 1)
        dve.wait_ge(const_done, 2)
        dve.wait_ge(alibi_done, 1)
        for i in reversed(range(NH)):
            last = nc.vector.tensor_scalar(alibi[:, i, :], alibi[:, 0, :], SLOPES[i], MAX_BIAS, ALU.mult, ALU.min)

        def step(b, p):
            if alive(b, BATCH):
                if not isinstance(b, int) or b >= 2:
                    dve.wait_ge(tr_done, b - 1)
                for u in range(QT):
                    last = nc.vector.tensor_scalar(h[:, p, u, :], x[:, 2 * b + u, :], mean[:, bass.ds(2 * b + u, 1)],
                                                   rstd[:, bass.ds(2 * b + u, 1)], ALU.subtract, ALU.mult)
                last.then_inc(ln_done, 1)
            c, q = b - 3, 1 - p
            if alive(c, BATCH):
                dve.wait_ge(exp_done, c + 1)
                nc.vector.reciprocal(rinv[:, q, :], rowsum[:, q, :]).then_inc(rinv_done, 1)
                dve.wait_ge(rinv_done, c + 1)
                dve.wait_ge(pv_mm, c + 1)
                for u in range(QT):
                    nc.vector.scalar_tensor_tensor(out=x[:, 2 * c + u, :], in0=bank[6 + q][:, P * u:P * u + P],
                                                   scalar=rinv[:, q, u:u + 1], in1=x[:, 2 * c + u, :],
                                                   op0=ALU.mult, op1=ALU.add).then_inc(att_done, 1)
                for u in range(QT):
                    dve.wait_ge(att_done, 2 * c + u + 1)
                    nc.vector.bn_stats(stats[:, 2 * c + u, :], x[:, 2 * c + u, :]).then_inc(stats_done, 1)
            c, q = b - 1, 1 - p
            if alive(c, BATCH):
                dve.wait_ge(s_mm, c + 1)
                if alive(c - 2, BATCH):
                    dve.wait_ge(exp_done, c - 1)
                nc.vector.scalar_tensor_tensor(out=scores[:, q], in0=bank[3 + q][:].rearrange("p (u k) -> p u k", u=QT),
                                               scalar=float(D) ** -0.5, in1=keep[:], op0=ALU.mult,
                                               op1=ALU.mult).then_inc(s_read, 1)
                dve.wait_ge(s_read, c + 1)
                nc.vector.tensor_scalar(zeros_masked[:], scores[:, q], 0.0, NEG, ALU.is_equal,
                                        ALU.mult).then_inc(mask_a, 1)
                wait_apart(dve, (mask_a, c + 1))
                for u in range(QT):
                    last = nc.vector.tensor_tensor_reduce(scores[:, q, u, :], scores[:, q, u, :], zeros_masked[:, u, :],
                                                          -1.0, 3e38, ALU.add, ALU.min, negmax[:, q, u:u + 1])
                last.then_inc(mask_done, 1)

        pipelined(dve, step, BATCH, 3, 4)

        dve.wait_ge(stats_done, NT // 4 + NT)
        norm_stats()
        dve.wait_ge(var_done, 2)
        dve.wait_ge(rstd_done, 2)
        link(nc.vector.tensor_scalar(ln_tmp[:, 0, :], ln_tmp[:, 3, :], 1.0 / D, None, ALU.mult))
        link(nc.vector.tensor_tensor(ln_tmp[:, 0, :], ln_tmp[:, 0, :], rstd[:], ALU.mult))
        link(nc.vector.tensor_tensor(ln_tmp[:, 0, :], ln_tmp[:, 0, :], rstd[:], ALU.mult))
        nc.vector.tensor_scalar(r_rms, ln_tmp[:, 0, :], RMS_EPS, None, ALU.add).then_inc(ms_done, 1)

        def norm4(g, p):
            if alive(g, NG):
                if alive(g - 2, NG):
                    dve.wait_ge(tr4_done, g - 1)
                    dve.wait_ge(xf_done, g - 1)
                for j in range(GT):
                    last = nc.vector.tensor_scalar(h4[:, p, j, :], x[:, GT * g + j, :], mean[:, bass.ds(GT * g + j, 1)],
                                                   rstd[:, bass.ds(GT * g + j, 1)], ALU.subtract, ALU.mult)
                last.then_inc(h4_done, 1)
            c, q = g - 1, 1 - p
            if alive(c, NG):
                dve.wait_ge(tr4_done, c + 1)
                if alive(c - 2, NG):
                    dve.wait_ge(router_mm, c - 1)
                    dve.wait_ge(xfT_done, c - 1)
                nc.vector.tensor_copy(xf_tile[:, q, :], bank[q][:]).then_inc(xft_done, 1)

        pipelined(dve, norm4, NG, 1, 4)

        def first_max(values, n, onehot, index, best):
            eq, cand = rt[4], rt[5]
            link(nc.vector.tensor_reduce(best, values, AX, ALU.max))
            link(nc.vector.tensor_tensor(eq, values, best.unsqueeze(2).to_broadcast([P, NT, E0]), ALU.is_equal))
            link(nc.vector.scalar_tensor_tensor(out=cand, in0=eq, scalar=-float(E0), in1=iota_e[:], op0=ALU.mult, op1=ALU.add))
            link(nc.vector.tensor_reduce(index, cand, AX, ALU.min))
            link(nc.vector.tensor_scalar(index, index, float(E0), None, ALU.add))
            link(nc.vector.tensor_tensor(onehot, iota_e[:], index.unsqueeze(2).to_broadcast([P, NT, E0]), ALU.is_equal))

        def ranks(out, counted):
            totals, upto = rt[4], rt[5]
            dve.wait_ge(counted, 1)
            link(nc.vector.tensor_copy(totals, bank[7][:, 256:512].rearrange("p (t e) -> p t e", e=E0)))
            for e in range(E0):
                last = nc.vector.tensor_tensor_scan(upto[:, :, e], ones_t[:], totals[:, :, e], 0.0, ALU.mult, ALU.add)
            link(last)
            link(nc.vector.tensor_tensor(out, upto, totals, ALU.subtract))
            link(nc.vector.tensor_tensor(out, out, bank[7][:, 0:256].rearrange("p (t e) -> p t e", e=E0), ALU.add))

        dve.wait_ge(router_mm, NG)
        dve.wait_ge(rms_done, 1)
        dve.wait_ge(const_done, 3)
        logits, rest, rank = rt[0], rt[1], rt[2]
        link(nc.vector.tensor_tensor(logits, bank[6][:, 0:256].rearrange("p (t e) -> p t e", e=E0),
                                     r_rms.unsqueeze(2).to_broadcast([P, NT, E0]), ALU.mult))
        first_max(logits, 0, oh[:, 0], rs[0], rs[1])
        link(nc.vector.scalar_tensor_tensor(out=rest, in0=oh[:, 0], scalar=-BIG, in1=logits, op0=ALU.mult, op1=ALU.add))
        first_max(rest, 1, oh[:, 1], rs[2], rs[3])
        nc.vector.tensor_tensor(rs[4], rs[3], rs[1], ALU.subtract).then_inc(d12_done, 1)
        nc.vector.tensor_tensor(picked_b, oh[:, 0], oh[:, 1], ALU.add).then_inc(picked, 1)
        dve.wait_ge(e2_done, 1)
        link(nc.vector.tensor_scalar(rs[6], rs[5], 1.0, None, ALU.add))
        link(nc.vector.reciprocal(rs[7], rs[6]))
        weight = rk[0]
        nc.vector.tensor_copy(weight[:, :, 0], rs[7])
        link(nc.vector.tensor_tensor(weight[:, :, 1], rs[5], rs[7], ALU.mult))
        ranks(rank, count_mm)
        mine = rk[1]
        for k in range(2):
            link(nc.vector.tensor_tensor(rt[3], oh[:, k], rank, ALU.mult))
            link(nc.vector.tensor_reduce(mine[:, :, k], rt[3], AX, ALU.add))
        fits, goes, back = rk[2], rk[3], rk[4]
        link(nc.vector.tensor_scalar(fits, mine, float(CAP), None, ALU.is_lt))
        for k in range(2):
            last = nc.vector.scalar_tensor_tensor(out=goes[:, :, k], in0=rs[2 * k], scalar=float(CAP), in1=mine[:, :, k],
                                                  op0=ALU.mult, op1=ALU.add)
        link(last)
        link(nc.vector.tensor_scalar(back, goes, -float(SLOTS), None, ALU.add))
        link(nc.vector.tensor_tensor(back, back, fits, ALU.mult))
        link(nc.vector.tensor_scalar(back, back, float(SLOTS), None, ALU.add))
        link(nc.vector.tensor_tensor(goes, goes, spare_slot[:], ALU.subtract))
        link(nc.vector.tensor_tensor(goes, goes, fits, ALU.mult))
        link(nc.vector.tensor_tensor(goes, goes, spare_slot[:], ALU.add))
        nc.vector.tensor_copy(slot_back[:], back)
        nc.vector.tensor_tensor(gate_w[:], weight, fits, ALU.mult)
        nc.vector.tensor_copy(slot[:], goes).then_inc(slots_done, 1)

        def product(n, k, out, free):
            dve.wait_ge(sil_done, n + 1)
            if free is not None:
                dve.wait_ge(down_mm, free)
            nc.vector.tensor_tensor(out, sil[:, k, 0:out.shape[1]], bank[4 + k][:, 0:out.shape[1]], ALU.mult).then_inc(hid_done, 1)

        def shared(g, p):
            for c in range(8):
                if alive(g, NG):
                    product(8 * g + c, c % 2, hidden[:, p, c, :], g - 1 if alive(g - 2, NG) else None)
                d, q = g - 1, 1 - p
                if c == 4 and alive(d, NG):
                    dve.wait_ge(down_mm, d + 1)
                    xs = x[:, bass.ds(GT * d, GT), :]
                    nc.vector.tensor_tensor(xs, bank[6 + q][:].rearrange("p (j d) -> p j d", d=D), xs, ALU.add).then_inc(down_read, 1)

        pipelined(dve, shared, NG, 1, 4)

        def routed(s, p):
            e, q = s - 1, 1 - p
            for k in range(8):
                if alive(e, E0):
                    c, half = k // 2, k % 2
                    product(8 * NG + 8 * e + k, half, hidden_e(q)[:, c, HALF * half:HALF * half + HALF], NG + e - 1 if alive(e - 2, E0) else NG)
                d = s - 2
                if k == 4 and alive(d, E0):
                    dve.wait_ge(down_mm, NG + d + 1)
                    if alive(d - 2, E0):
                        dve.wait_ge(eo_out[p], eo_count(d, p))
                    nc.vector.tensor_copy(eo[:, p, 0:4, :], bank[6][:].rearrange("p (j d) -> p j d", d=D))
                    nc.vector.tensor_copy(eo[:, p, 4, :], bank[7][:, 0:P]).then_inc(down_read, 1)

        pipelined(dve, routed, E0, 2, 4)

        dve.wait_ge(w3_in, 80)
        link(nc.vector.tensor_scalar(bqk[:, 0:1], bqk[:, 0:1], QK_SCALE, None, ALU.mult))
        link(nc.vector.memset(v3.rearrange("p b u h d -> p (b u h d)"), 1.0))

        def prenorm(b, p):
            dve.wait_ge(given_in[p], 32 * (b - p) + 64)
            for k in range(2):
                if k == 1:
                    dve.wait_ge(comb_a, 2 * b + 2)
                for u in range(QT):
                    last = nc.vector.scalar_tensor_tensor(out=x[:, 2 * b + u, :], in0=given[:, p, 2 * u + k, :],
                                                          scalar=gate_w[:, 2 * b + u, k:k + 1], in1=x[:, 2 * b + u, :],
                                                          op0=ALU.mult, op1=ALU.add)
                    if k == 0:
                        last.then_inc(comb_a, 1)
            last.then_inc(comb_done, 1)
            wait_apart(dve, (comb_done, b + 1), *([(rstd3_done, b - 1)] if alive(b - 2, BATCH) else []))
            for u in range(QT):
                last = nc.vector.bn_stats(bn3[:, p, u, :], x[:, 2 * b + u, :])
            last.then_inc(st_a, 1)
            wait_apart(dve, (st_a, b + 1))
            for u in range(QT):
                last = nc.vector.bn_aggr(mv[:, p, u, 0:2], bn3[:, p, u, :])
            last.then_inc(st_b, 1)
            dve.wait_ge(st_b, b + 1)
            nc.vector.tensor_scalar(mv[:, p, :, 2], mv[:, p, :, 1], LN_EPS, None, ALU.add).then_inc(var3_done, 1)

        def norm3(b, p):
            dve.wait_ge(rstd3_done, b + 1)
            if alive(b - 2, BATCH):
                dve.wait_ge(tr3, b - 1)
            for u in range(QT):
                last = nc.vector.tensor_scalar(h3[:, p, u, :], x[:, 2 * b + u, :], mv[:, p, u, 0:1], rstd3[:, p, u:u + 1],
                                               ALU.subtract, ALU.mult)
            last.then_inc(h3_done, 1)

        def values(b, p):
            dve.wait_ge(v3_mm, b + 1)
            if alive(b - 2, BATCH):
                dve.wait_ge(pv3_mm, NH // HG * (b - 1))
            for u in range(QT):
                last = nc.vector.tensor_tensor(v3[:, p, u, :, 0:HD], bank[6][:, SEQ + D * u:SEQ + D * u + D].rearrange("p (h d) -> p h d", d=HD),
                                               bv[:].rearrange("p (h d) -> p h d", d=HD), ALU.add)
            last.then_inc(v3_done, 1)

        def divide(e, u):
            sums = bank[5][:].rearrange("p (n d) -> p n d", d=TILE)
            dve.wait_ge(ob_tr, QT * e + u + 1)
            nc.vector.reciprocal(rinv3[:, u], sums[:, :, HD]).then_inc(rinv3_done, 1)
            if u == 0 and alive(e - 1, BATCH):
                dve.wait_ge(oT3_tr, e)
            dve.wait_ge(rinv3_done, QT * e + u + 1)
            nc.vector.tensor_tensor(o3[:, u].rearrange("p (h d) -> p h d", d=HD), sums[:, :, 0:HD],
                                    rinv3[:, u].unsqueeze(2).to_broadcast([P, NH, HD]), ALU.mult).then_inc(o3_done, 1)

        def residual(e, p):
            dve.wait_ge(out3_mm, e + 1)
            xs = x[:, bass.ds(2 * e, QT), :]
            nc.vector.tensor_tensor(xs, bank[7][:, 0:SEQ].rearrange("p (u d) -> p u d", d=D), xs, ALU.add).then_inc(res3_a, 1)
            dve.wait_ge(res3_a, 2 * e + 1)
            nc.vector.tensor_tensor(xs, xs, bo[:].unsqueeze(1).to_broadcast([P, QT, D]), ALU.add).then_inc(res3_a, 1)
            wait_apart(dve, (res3_a, 2 * e + 2))
            for u in range(QT):
                last = nc.vector.bn_stats(stats[:, 2 * e + u, :], x[:, 2 * e + u, :])
            last.then_inc(res3_done, 1)

        def heads(b, p):
            for h in range(NH):
                c, q, hh, n = item(b, p, h, 1)
                if alive(c, BATCH):
                    wait_apart(dve, (s3_mm, n + 1), *([(exp3_done, n - 3)] if not isinstance(n, int) or n >= 4 else []))
                    for u in range(QT):
                        last = nc.vector.tensor_tensor_reduce(sc3[:, hh % 4, u, :], bank[hh % 2][:, SEQ * u:SEQ * u + SEQ],
                                                              alibi[:, hh, P * (1 - u):P * (1 - u) + SEQ], -1.0, BIG,
                                                              ALU.add, ALU.min, nmax3[:, hh % 4, u:u + 1])
                    last.then_inc(max3_done, 1)
                c, q, hh, n = item(b, p, h, 4)
                if alive(c, BATCH) and hh in DVE_COPIES:
                    dve.wait_ge(pT3_tr, n + 1)
                    place_used(dve, c, hh)
                    nc.vector.tensor_copy(prT3[:, hh % (2 * HG)].rearrange("p k t -> p (k t)"), bank[2 + hh % 2][:]).then_inc(copied_d, 1)
                c, q, hh, n = item(b, p, h, 6)
                if alive(c, BATCH) and hh % HG == HG - 1:
                    keep_group(dve, c, hh // HG)
                if h == 5 and alive(b, BATCH):
                    values(b, p)
                if h == 10 and alive(b + 1, BATCH):
                    prenorm(b + 1, 1 - p)
                if h == 14 and alive(b + 1, BATCH):
                    norm3(b + 1, 1 - p)
                if h in (7, 9) and alive(b - 2, BATCH):
                    divide(b - 2, (h - 7) // 2)
                if h == 13 and alive(b - 2, BATCH):
                    residual(b - 2, p)

        prenorm(0, 0)
        norm3(0, 0)
        pipelined(dve, heads, BATCH, 2, 4, ahead=2)
        if STAGE < 4:
            return

        dve.wait_ge(res3_done, BATCH)
        norm_stats()
        dve.wait_ge(gate_in, 48)
        link(nc.vector.tensor_tensor(wg_all[:], wg_all[:], wg_all[:], ALU.mult))
        nc.vector.tensor_reduce(inv_norm[:], wg_all[:], AX, ALU.add).then_inc(sq_done, 1)
        dve.wait_ge(gate_mm, 1)
        nc.vector.tensor_copy(w_gate[:], bank[7][:, 0:E1]).then_inc(gate_done, 1)
        dve.wait_ge(norm_root, 1)
        link(nc.vector.tensor_scalar(inv_norm[:], inv_norm[:], 1e-4, None, ALU.max))
        link(nc.vector.reciprocal(inv_norm[:], inv_norm[:]))
        dve.wait_ge(rstd_done, 3)

        def norm5(g, p):
            if alive(g, NG):
                if alive(g - 2, NG):
                    dve.wait_ge(tr5, g - 1)
                for j in range(GT):
                    last = nc.vector.tensor_scalar(h5[:, p, j, :], x[:, GT * g + j, :], mean[:, bass.ds(GT * g + j, 1)],
                                                   rstd[:, bass.ds(GT * g + j, 1)], ALU.subtract, ALU.mult)
                last.then_inc(h5_done, 1)
            c, q = g - 1, 1 - p
            if alive(c, NG):
                dve.wait_ge(tr5, c + 1)
                if alive(c - 2, NG):
                    dve.wait_ge(router5_mm, c - 1)
                nc.vector.tensor_copy(h5T[:, q, :], bank[q][:]).then_inc(h5T_done, 1)

        pipelined(dve, norm5, NG, 1, 4)

        dve.wait_ge(router5_mm, NG)
        logits, less, rank = rt[0], rt[1], rt[2]
        link(nc.vector.tensor_tensor(logits, bank[6][:, 0:256].rearrange("p (t e) -> p t e", e=E1),
                                     inv_norm[:].unsqueeze(1).to_broadcast([P, NT, E1]), ALU.mult))
        first_max(logits, 0, oh[:, 0], rs[0], rs[1])
        nc.vector.tensor_copy(picked_b, oh[:, 0]).then_inc(picked5, 1)
        nc.vector.tensor_tensor(less, logits, rs[1].unsqueeze(2).to_broadcast([P, NT, E1]), ALU.subtract).then_inc(less_done, 1)
        ranks(rank, count5_mm)
        counts, first, upto = tile_rs[:, 0], tile_rs[:, 1], tile_rs[:, 2]
        link(nc.vector.tensor_scalar(counts, rt[5][:, NT - 1, :], float(P - 1), None, ALU.add))
        link(nc.vector.tensor_copy(n_int[:], counts))
        link(nc.vector.tensor_scalar(n_int[:], n_int[:], P.bit_length() - 1, None, ALU.arith_shift_right))
        link(nc.vector.tensor_copy(counts, n_int[:]))
        link(nc.vector.tensor_tensor_scan(upto, ones_t[:, 0:E1], counts, 0.0, ALU.mult, ALU.add))
        link(nc.vector.tensor_tensor(first, upto, counts, ALU.subtract))
        link(nc.vector.tensor_scalar(upto, first, float(P), None, ALU.mult))
        link(nc.vector.tensor_tensor(rank, rank, upto.unsqueeze(1).to_broadcast([P, NT, E1]), ALU.add))
        link(nc.vector.tensor_tensor(rank, rank, oh[:, 0], ALU.mult))
        link(nc.vector.tensor_reduce(rs[2], rank, AX, ALU.add))
        nc.vector.tensor_copy(slot5[:], rs[2])
        tiles = tile_no[:]
        link(nc.vector.tensor_tensor(tiles, tiles, first.unsqueeze(1).to_broadcast([P, TILES, E1]), ALU.is_ge))
        link(nc.vector.tensor_reduce(owner, tiles, AX, ALU.add))
        nc.vector.tensor_scalar(tile_expert[:], owner, -1.0, None, ALU.add)
        dve.wait_ge(exp5_done, 1)
        link(nc.vector.tensor_reduce(rs[3], less, AX, ALU.add))
        nc.vector.reciprocal(extra[:, :, 1], rs[3])
        nc.vector.tensor_copy(extra[:, :, 0], token_no[:])
        nc.vector.tensor_copy(extra[:, :, 2], mean[:])
        nc.vector.tensor_copy(extra[:, :, 3], rstd[:]).then_inc(slots5_done, 1)
        dve.wait_ge(w_all_in, 64)
        dve.wait_ge(slots5_done, 1)

        def tile_step(j, p):
            if alive(j, TILES):
                if alive(j - 4, TILES):
                    dve.wait_ge(y_done, j - 3)
                e = dve.value_load(tile_expert[0:1, bass.ds(j, 1)], min_val=0, max_val=E1 - 1)
                nc.vector.tensor_copy(w_own[:, p], w_all[:, bass.ds(e, 1), :].rearrange("p a w -> p (a w)")).then_inc(own_done, 1)
                dve.wait_ge(xr_in[p], 4 * (j - p) + 16)
                if alive(j - 2, TILES):
                    dve.wait_ge(trj, j - 1)
                nc.vector.tensor_scalar(hj[:, p % 2], xr[:, p, 0:D], xr[:, p, D + 2:D + 3], xr[:, p, D + 3:D + 4],
                                        ALU.subtract, ALU.mult).then_inc(hj_done, 1)
            c, q, q2 = j - 3, (p + 1) % 4, (p + 1) % 2
            if alive(c, TILES):
                dve.wait_ge(down5_mm, c + 1)
                nc.vector.tensor_tensor(yj[:, q2], bank[4 + q2][:, 0:D], w_own[:, q, 2 * I1 + I1 // P:W_ALL], ALU.add).then_inc(y_done, 1)
                if alive(c - 2, TILES):
                    dve.wait_ge(stored[q2], 8 * (c - q2))
                dve.wait_ge(y_done, c + 1)
                nc.vector.tensor_copy(token[:, q2], xr[:, q, D:D + 1])
                nc.vector.scalar_tensor_tensor(out=rj[:, q2], in0=yj[:, q2], scalar=xr[:, q, D + 1:D + 2],
                                               in1=xr[:, q, 0:D], op0=ALU.mult, op1=ALU.add).then_inc(rj_done, 1)

        pipelined(dve, tile_step, TILES, 3, 8, 4)

    @block.scalar
    def _(act):
        def step(b, p):
            c = b - 2
            if alive(c, BATCH):
                act.wait_ge(mask_done, c + 1)
                if alive(c - 2, BATCH):
                    act.wait_ge(pT_tr, c - 1)
                    act.wait_ge(rinv_done, c - 1)
                for u in range(QT):
                    last = nc.scalar.activation(probs[:, p, u, :], scores[:, p, u, :], ACT.Exp, scale=-1.0,
                                                bias=negmax[:, p, u:u + 1], accum_out=rowsum[:, p, u:u + 1])
                last.then_inc(exp_done, 1)
            if alive(b, BATCH):
                act.wait_ge(tr_done, b + 1)
                if alive(b - 2, BATCH):
                    act.wait_ge(v_mm, b - 1)
                nc.scalar.activation(hT[:, p], psum_T(p), ACT.Copy).then_inc(hT_done, 1)
            if alive(c, BATCH):
                act.wait_ge(pT_tr, c + 1)
                if alive(c - 1, BATCH):
                    act.wait_ge(pv_mm, c)
                nc.scalar.activation(probsT[:].rearrange("p u k -> p (u k)"), bank[5][:], ACT.Copy).then_inc(pT_done, 1)
            if alive(b, BATCH):
                act.wait_ge(qk_mm, b + 1)
                if alive(b - 2, BATCH):
                    act.wait_ge(s_mm, b - 1)
                nc.scalar.activation(qk[:, p].rearrange("p a k -> p (a k)"), bank[1][:], ACT.Copy).then_inc(qk_done, 1)
                act.wait_ge(v_mm, b + 1)
                if alive(b - 2, BATCH):
                    act.wait_ge(pv_mm, b - 1)
                nc.scalar.activation(v[:, p].rearrange("p u d -> p (u d)"), psum_V(p), ACT.Copy).then_inc(v_done, 1)

        pipelined(act, step, BATCH, 2, 4)

        def keep_xT(g, p):
            act.wait_ge(xft_done, g + 1)
            nc.scalar.activation(xfT[:, bass.ds(GT * P * g, GT * P)], xf_tile[:, p], ACT.Copy).then_inc(xfT_done, 1)

        pipelined(act, keep_xT, NG, 0)
        act.wait_ge(d12_done, 1)
        nc.scalar.activation(rs[5], rs[4], ACT.Exp).then_inc(e2_done, 1)

        def silu(n, k, width):
            act.wait_ge(gu_mm, n + 1)
            if not isinstance(n, int) or n >= 2:
                act.wait_ge(hid_done, n - 1)
            nc.scalar.activation(sil[:, k, 0:width], bank[2 + k][:, 0:width], ACT.Silu).then_inc(sil_done, 1)

        def shared(g, p):
            for c in range(8):
                silu(8 * g + c, c % 2, GT * P)

        pipelined(act, shared, NG, 0)

        def routed(s, p):
            if alive(s, E0):
                act.wait_ge(xg_tr, s + 1)
                if alive(s - 2, E0):
                    act.wait_ge(gu_mm, 8 * NG + 8 * (s - 1))
                nc.scalar.activation(xgT[:, p, 0:512], bank[0][:], ACT.Copy)
                nc.scalar.activation(xgT[:, p, 512:CAP], bank[1][:, 0:P], ACT.Copy).then_inc(xgT_done, 1)
            e = s - 1
            if alive(e, E0):
                for k in range(8):
                    silu(8 * NG + 8 * e + k, k % 2, HALF)

        pipelined(act, routed, E0, 1, 4)

        def heads(b, p):
            for h in range(NH):
                c, q, hh, n = item(b, p, h, 2)
                if alive(c, BATCH):
                    if not isinstance(n, int) or n >= 4:
                        act.wait_ge(pT3_tr, n - 3)
                    act.wait_ge(max3_done, n + 1)
                    for u in range(QT):
                        last = nc.scalar.activation(pr3[:, hh % 4, u, :], sc3[:, hh % 4, u, :], ACT.Exp, scale=-1.0,
                                                    bias=nmax3[:, hh % 4, u:u + 1])
                    last.then_inc(exp3_done, 1)
                c, q, hh, n = item(b, p, h, 4)
                if alive(c, BATCH) and hh not in DVE_COPIES:
                    act.wait_ge(pT3_tr, n + 1)
                    place_used(act, c, hh)
                    nc.scalar.activation(prT3[:, hh % (2 * HG)].rearrange("p k t -> p (k t)"), bank[2 + hh % 2][:], ACT.Copy).then_inc(copied_a, 1)
                if h == 0 and alive(b, BATCH):
                    act.wait_ge(tr3, b + 1)
                    if alive(b - 1, BATCH):
                        act.wait_ge(v3_mm, b)
                    nc.scalar.activation(hT3, bank[6][:, 0:SEQ], ACT.Copy).then_inc(hT3_done, 1)
                if h == 2 and alive(b, BATCH):
                    act.wait_ge(qk3_mm, b + 1)
                    if alive(b - 1, BATCH):
                        act.wait_ge(parts_done, b)
                    nc.scalar.activation(qkf[:, 0], bank[7][:, 0:SEQ], ACT.Identity, scale=QK_SCALE, bias=bqk[:, 0:1])
                    nc.scalar.activation(qkf[:, 1], bank[7][:, SEQ:2 * SEQ], ACT.Identity, bias=bqk[:, 1:2]).then_inc(qk3_done, 1)
                if h == 11 and alive(b - 2, BATCH):
                    act.wait_ge(oT3_tr, b - 1)
                    if alive(b - 3, BATCH):
                        act.wait_ge(out3_mm, b - 2)
                    nc.scalar.activation(oT3, bank[6][:, 0:SEQ], ACT.Copy).then_inc(oT3_done, 1)

        pipelined(act, heads, BATCH, 2, 4)
        if STAGE < 4:
            return
        act.wait_ge(less_done, 1)
        nc.scalar.activation(rt[1], rt[1], ACT.Exp).then_inc(exp5_done, 1)

        def tile_step(j, p):
            if alive(j, TILES):
                act.wait_ge(trj, j + 1)
                if alive(j - 2, TILES):
                    act.wait_ge(up_mm, j - 1)
                nc.scalar.activation(hjT[:, p % 2], bank[p % 2][:, 0:P], ACT.Copy).then_inc(hjT_done, 1)
            c, q, q2 = j - 1, (p - 1) % 4, (p - 1) % 2
            if alive(c, TILES):
                act.wait_ge(up_mm, c + 1)
                if alive(c - 2, TILES):
                    act.wait_ge(down5_mm, c - 1)
                for f in range(I1 // P):
                    last = nc.scalar.activation(gj[:, q2, f, :], bank[2 + q2][:, P * f:P * f + P], ACT.Gelu,
                                                bias=w_own[:, q, 2 * I1 + f:2 * I1 + f + 1])
                last.then_inc(gelu_done, 1)

        pipelined(act, tile_step, TILES, 1, 4, 4)

    @block.tensor
    def _(pe):
        pe.wait_ge(const_done, 2)
        pe.wait_ge(w_in, 16)

        def step(b, p):
            if alive(b, BATCH):
                pe.wait_ge(ln_done, b + 1)
                if alive(b - 2, BATCH):
                    pe.wait_ge(hT_done, b - 1)
                for u in range(QT):
                    last = nc.tensor.transpose(psum_T(p)[:, P * u:P * u + P], h[:, p, u, :], ident[:])
                last.then_inc(tr_done, 1)
            c, q = b - 1, 1 - p
            if alive(c, BATCH):
                pe.wait_ge(qk_done, c + 1)
                if alive(c - 2, BATCH):
                    pe.wait_ge(s_read, c - 1)
                for u in range(QT):
                    last = nc.tensor.matmul(bank[3 + q][:, SEQ * u:SEQ * u + SEQ], qk[:, q, 0, P * u:P * u + P],
                                            qk[:, q, 1, :], start=True, stop=True)
                last.then_inc(s_mm, 1)
            c = b - 2
            if alive(c, BATCH):
                pe.wait_ge(exp_done, c + 1)
                if alive(c - 1, BATCH):
                    pe.wait_ge(pT_done, c)
                for k in range(QT):
                    for u in range(QT):
                        last = nc.tensor.transpose(bank[5][:, SEQ * k + P * u:SEQ * k + P * u + P],
                                                   probs[:, p, u, P * k:P * k + P], ident[:])
                last.then_inc(pT_tr, 1)
            if alive(b, BATCH):
                pe.wait_ge(hT_done, b + 1)
                if alive(b - 1, BATCH):
                    pe.wait_ge(qk_done, b)
                for a in range(2):
                    last = nc.tensor.matmul(bank[1][:, SEQ * a:SEQ * a + SEQ], wqkv[:, D * a:D * a + D], hT[:, p],
                                            start=True, stop=True)
                last.then_inc(qk_mm, 1)
                if alive(b - 2, BATCH):
                    pe.wait_ge(v_done, b - 1)
                for u in range(QT):
                    last = nc.tensor.matmul(psum_V(p)[:, P * u:P * u + P], hT[:, p, P * u:P * u + P],
                                            wqkv[:, 2 * D:3 * D], start=True, stop=True)
                last.then_inc(v_mm, 1)
            c = b - 2
            if alive(c, BATCH):
                pe.wait_ge(pT_done, c + 1)
                pe.wait_ge(v_done, c + 1)
                if alive(c - 2, BATCH):
                    pe.wait_ge(att_done, QT * (c - 1))
                for u in range(QT):
                    for k in range(QT):
                        last = nc.tensor.matmul(bank[6 + p][:, P * u:P * u + P], probsT[:, k, P * u:P * u + P],
                                                v[:, p, k, :], start=(k == 0), stop=(k == QT - 1))
                last.then_inc(pv_mm, 1)

        pipelined(pe, step, BATCH, 2, 4)

        pe.wait_ge(w_router_in, 16)

        def route(g, p):
            if alive(g, NG):
                pe.wait_ge(h4_done, g + 1)
                if alive(g - 2, NG):
                    pe.wait_ge(xft_done, g - 1)
                for j in range(GT):
                    last = nc.tensor.transpose(bank[p][:, P * j:P * j + P], h4[:, p, j, :], ident[:])
                last.then_inc(tr4_done, 1)
            c, q = g - 1, 1 - p
            if alive(c, NG):
                pe.wait_ge(xft_done, c + 1)
                for j in range(GT):
                    last = nc.tensor.matmul(bank[6][:, bass.ds(E0 * (GT * c + j), E0)], xf_tile[:, q, P * j:P * j + P],
                                            w_router, start=True, stop=True)
                last.then_inc(router_mm, 1)

        pipelined(pe, route, NG, 1, 4)

        def count(counted):
            nc.tensor.matmul(bank[7][:, 0:256], upper[:], picked_b.rearrange("p t e -> p (t e)"), start=True, stop=True)
            nc.tensor.matmul(bank[7][:, 256:512], ones_b[:], picked_b.rearrange("p t e -> p (t e)"),
                             start=True, stop=True).then_inc(counted, 1)

        pe.wait_ge(w_shared_in, 48)

        def gate_up(n, k, width, wg, wu, rhs):
            if not isinstance(n, int) or n >= 2:
                pe.wait_ge(hid_done, n - 1)
            nc.tensor.matmul(bank[2 + k][:, 0:width], wg, rhs, start=True, stop=True)
            nc.tensor.matmul(bank[4 + k][:, 0:width], wu, rhs, start=True, stop=True).then_inc(gu_mm, 1)

        def shared(g, p):
            for c in range(8):
                if alive(g, NG):
                    if c == 0:
                        pe.wait_ge(xfT_done, g + 1)
                    gate_up(8 * g + c, c % 2, 512, w_sg[:, P * c:P * c + P], w_su[:, P * c:P * c + P],
                            xfT[:, bass.ds(512 * g, 512)])
                if isinstance(g, int) and g == 0 and c == 1:
                    pe.wait_ge(picked, 1)
                    count(count_mm)
                d, q = g - 1, 1 - p
                if c == 1 and alive(d, NG):
                    pe.wait_ge(hid_done, 8 * (d + 1))
                    if alive(d - 2, NG):
                        pe.wait_ge(down_read, d - 1)
                    elif d == 1:
                        pe.wait_ge(slots_done, 1)
                    for j in range(GT):
                        for f in range(8):
                            last = nc.tensor.matmul(bank[6 + q][:, D * j:D * j + D], hidden[:, q, f, P * j:P * j + P],
                                                    w_sd[:, f, :], start=(f == 0), stop=(f == 7))
                    last.then_inc(down_mm, 1)

        pipelined(pe, shared, NG, 1, 4)

        def routed(s, p):
            if alive(s, E0):
                pe.wait_ge(xg_in[p], 8 * (s - p) + 16)
                if alive(s - 1, E0):
                    pe.wait_ge(xgT_done, s)
                for j in range(CT):
                    last = nc.tensor.transpose(bank[j // 4][:, P * (j % 4):P * (j % 4) + P], xg[:, p, j, :], ident[:])
                last.then_inc(xg_tr, 1)
            e, q = s - 1, 1 - p
            for k in range(8):
                if alive(e, E0):
                    c, half = k // 2, k % 2
                    if k == 0:
                        pe.wait_ge(xgT_done, e + 1)
                        pe.wait_ge(ew_in[q], 24 * (e - q) + 48)
                    gate_up(8 * NG + 8 * e + k, half, HALF, w_eg[:, q, P * c:P * c + P], w_eu[:, q, P * c:P * c + P],
                            xgT[:, q, HALF * half:HALF * half + HALF])
                d = s - 2
                if k == 1 and alive(d, E0):
                    pe.wait_ge(hid_done, 8 * NG + 8 * (d + 1))
                    pe.wait_ge(down_read, NG + d)
                    for j in range(CT):
                        for f in range(I0 // P):
                            last = nc.tensor.matmul(bank[6 + j // 4][:, D * (j % 4):D * (j % 4) + D],
                                                    hidden_e(p)[:, f, P * j:P * j + P], w_ed[:, p, f, :],
                                                    start=(f == 0), stop=(f == I0 // P - 1))
                    last.then_inc(down_mm, 1)

        pipelined(pe, routed, E0, 2, 4)

        pe.wait_ge(w3_in, 80)

        def turn(b, p):
            pe.wait_ge(h3_done, b + 1)
            if alive(b - 3, BATCH):
                pe.wait_ge(oT3_done, b - 2)
            if alive(b - 1, BATCH):
                pe.wait_ge(v3_done, b)
            for u in range(QT):
                last = nc.tensor.transpose(bank[6][:, P * u:P * u + P], h3[:, p, u, :], ident[:])
            last.then_inc(tr3, 1)

        def heads(b, p):
            for h in range(NH):
                c, q, hh, n = item(b, p, h, 0)
                if alive(c, BATCH):
                    if h == 0:
                        pe.wait_ge(qk3_in[q], 96 * (c - q) + 192)
                    if not isinstance(n, int) or n >= 2:
                        pe.wait_ge(max3_done, n - 1)
                    for u in range(QT):
                        last = nc.tensor.matmul(bank[h % 2][:, SEQ * u:SEQ * u + SEQ], qs[0:KROWS, q, h, P * u:P * u + P],
                                                ks[0:KROWS, q, h, :], start=True, stop=True)
                    last.then_inc(s3_mm, 1)
                c, q, hh, n = item(b, p, h, 3)
                if alive(c, BATCH):
                    pe.wait_ge(exp3_done, n + 1)
                    c2, _, h2, n2 = item(b, p, h, 5)
                    if alive(c2, BATCH):
                        pe.wait_ge(*copier(c2, h2))
                    for k in range(QT):
                        for u in range(QT):
                            last = nc.tensor.transpose(bank[2 + hh % 2][:, SEQ * k + P * u:SEQ * k + P * u + P],
                                                       pr3[:, hh % 4, u, P * k:P * k + P], ident[:])
                    last.then_inc(pT3_tr, 1)
                c, q, hh, n = item(b, p, h, 5)
                if alive(c, BATCH) and hh % HG == HG - 1:
                    g = hh // HG
                    for own in (True, False):
                        of_kind = [k for k in range(HG * g, HG * g + HG) if (k in DVE_COPIES) == own]
                        if of_kind:
                            pe.wait_ge(*copier(c, of_kind[-1]))
                    if g == 0:
                        pe.wait_ge(v3_done, c + 1)
                    if g > 0 or alive(c - 1, BATCH):
                        pe.wait_ge(po_copied, NH // HG * c + g)
                    for k in range(QT):
                        for j in range(HG):
                            last = nc.tensor.matmul(bank[4][TILE * j:TILE * j + TILE, 0:SEQ], v3[:, q, k, HG * g + j, :],
                                                    prT3[:, (HG * g + j) % (2 * HG), k, :], start=(k == 0), stop=(k == QT - 1))
                    last.then_inc(pv3_mm, 1)
                if h == 15 and alive(b + 1, BATCH):
                    turn(b + 1, 1 - p)
                if h == 1 and alive(b, BATCH):
                    pe.wait_ge(hT3_done, b + 1)
                    if alive(b - 3, BATCH):
                        pe.wait_ge(res3_a, 2 * (b - 3) + 1)
                    for a in range(2):
                        last = nc.tensor.matmul(bank[7][:, SEQ * a:SEQ * a + SEQ], w3[:, D * a:D * a + D], hT3, start=True, stop=True)
                    last.then_inc(qk3_mm, 1)
                    for u in range(QT):
                        last = nc.tensor.matmul(bank[6][:, SEQ + D * u:SEQ + D * u + D], hT3[:, P * u:P * u + P],
                                                w3[:, 2 * D:3 * D], start=True, stop=True)
                    last.then_inc(v3_mm, 1)
                e = b - 2
                if h in (6, 8) and alive(e, BATCH):
                    u = (h - 6) // 2
                    pe.wait_ge(po_copied, NH // HG * (e + 1))
                    if u > 0 or alive(e - 1, BATCH):
                        pe.wait_ge(o3_done, QT * e + u)
                    for g in range(NH // HG):
                        last = nc.tensor.transpose(bank[5][:, P * g:P * g + P], oTu[:, g, P * u:P * u + P], ident[:])
                    last.then_inc(ob_tr, 1)
                if h == 10 and alive(e, BATCH):
                    pe.wait_ge(o3_done, QT * (e + 1))
                    if alive(b, BATCH):
                        pe.wait_ge(v3_done, b + 1)
                    for u in range(QT):
                        last = nc.tensor.transpose(bank[6][:, P * u:P * u + P], o3[:, u, :], ident[:])
                    last.then_inc(oT3_tr, 1)
                if h == 12 and alive(e, BATCH):
                    pe.wait_ge(oT3_done, e + 1)
                    if alive(b, BATCH):
                        pe.wait_ge(qk3_done, b + 1)
                    for u in range(QT):
                        last = nc.tensor.matmul(bank[7][:, D * u:D * u + D], oT3[:, P * u:P * u + P], w_out[:], start=True, stop=True)
                    last.then_inc(out3_mm, 1)

        turn(0, 0)
        pipelined(pe, heads, BATCH, 2, 4, ahead=2)
        if STAGE < 4:
            return

        pe.wait_ge(res3_done, BATCH)
        pe.wait_ge(gate_in, 48)
        nc.tensor.matmul(bank[7][:, 0:E1], w_redT[:], wgT[:], start=True, stop=True).then_inc(gate_mm, 1)

        def route5(g, p):
            if alive(g, NG):
                pe.wait_ge(h5_done, g + 1)
                if alive(g - 2, NG):
                    pe.wait_ge(h5T_done, g - 1)
                for j in range(GT):
                    last = nc.tensor.transpose(bank[p][:, P * j:P * j + P], h5[:, p, j, :], ident[:])
                last.then_inc(tr5, 1)
            c, q = g - 1, 1 - p
            if alive(c, NG):
                if isinstance(c, int) and c == 0:
                    pe.wait_ge(gate_done, 1)
                pe.wait_ge(h5T_done, c + 1)
                for j in range(GT):
                    last = nc.tensor.matmul(bank[6][:, bass.ds(E1 * (GT * c + j), E1)], h5T[:, q, P * j:P * j + P],
                                            w_gate[:], start=True, stop=True)
                last.then_inc(router5_mm, 1)

        pipelined(pe, route5, NG, 1, 4)
        pe.wait_ge(picked5, 1)
        count(count5_mm)

        def tile_step(j, p):
            if alive(j, TILES):
                pe.wait_ge(hj_done, j + 1)
                if alive(j - 2, TILES):
                    pe.wait_ge(hjT_done, j - 1)
                nc.tensor.transpose(bank[p % 2][:, 0:P], hj[:, p % 2], ident[:]).then_inc(trj, 1)
            c, q, q2 = j - 1, (p - 1) % 4, (p - 1) % 2
            if alive(c, TILES):
                pe.wait_ge(hjT_done, c + 1)
                pe.wait_ge(own_done, c + 1)
                if alive(c - 2, TILES):
                    pe.wait_ge(gelu_done, c - 1)
                for f in range(I1 // P):
                    last = nc.tensor.matmul(bank[2 + q2][:, P * f:P * f + P], w_own[:, q, P * f:P * f + P], hjT[:, q2],
                                            start=True, stop=True)
                last.then_inc(up_mm, 1)
            c, q, q2 = j - 2, (p - 2) % 4, p % 2
            if alive(c, TILES):
                pe.wait_ge(gelu_done, c + 1)
                if alive(c - 2, TILES):
                    pe.wait_ge(y_done, c - 1)
                for f in range(I1 // P):
                    last = nc.tensor.matmul(bank[4 + q2][:, 0:D], gj[:, q2, f, :], w_own[:, q, I1 + D * f:I1 + D * f + D],
                                            start=(f == 0), stop=(f == I1 // P - 1))
                last.then_inc(down5_mm, 1)

        pipelined(pe, tile_step, TILES, 2, 4, 4)


_INS = ["L0_attn_x", "L0_attn_W", "L0_ffn_router_w", "L0_ffn_rg", "L0_ffn_ru", "L0_ffn_rd", "L0_ffn_sg", "L0_ffn_su",
        "L0_ffn_sd", "L1_attn_in_proj_weight", "L1_attn_in_proj_bias", "L1_attn_out_proj_weight",
        "L1_attn_out_proj_bias", "L1_ffn_w_red", "L1_ffn_wg", "L1_ffn_w1", "L1_ffn_b1", "L1_ffn_w2", "L1_ffn_b2"]


def layout(inputs):
    a = {n: np.asarray(inputs[n]) for n in _INS}
    a["L0_ffn_router_w"] = a["L0_ffn_router_w"].T
    w1, w2, b1 = (a.pop(f"L1_ffn_{n}") for n in ("w1", "w2", "b1"))
    a["w1"] = w1.transpose(1, 0, 2)
    a["w2"] = w2.reshape(E1, I1 // P, P, D).transpose(2, 0, 1, 3).reshape(P, E1, I1)
    a["b1"] = b1.reshape(E1, I1 // P, P).transpose(2, 0, 1)
    a["b2"] = a.pop("L1_ffn_b2")
    a["w_redT"] = a.pop("L1_ffn_w_red").T
    a["wg"] = a.pop("L1_ffn_wg")
    a["wgT"] = a["wg"].T
    w, b = a.pop("L1_attn_in_proj_weight"), a.pop("L1_attn_in_proj_bias")
    by_d = [i.reshape(NH, HD, *i.shape[1:]).swapaxes(0, 1).reshape(i.shape) for i in (w[:D], w[D:2 * D], b[:D], b[D:2 * D])]
    a["w3"] = np.concatenate([by_d[0], by_d[1], w[2 * D:]]).T
    a["bqk"] = np.stack(by_d[2:], axis=1)
    a["bv"] = b[2 * D:]
    a["w_out"] = a.pop("L1_attn_out_proj_weight").T
    a["bo"] = a.pop("L1_attn_out_proj_bias")
    return {n: np.ascontiguousarray(v) for n, v in a.items()}


OUT_SHAPE = (BATCH, SEQ, D)


def kernel(**inputs):
    import concourse.bacc as _bacc
    from concourse.bass_utils import run_bass_kernel_spmd as _run

    arrays = layout(inputs)
    nc = _bacc.Bacc("TRN2", target_bir_lowering=False, num_devices=1)
    t = {n: nc.dram_tensor(f"in_{n}", a.shape, mybir.dt.from_np(a.dtype), kind="ExternalInput").ap()
         for n, a in arrays.items()}
    t["out"] = nc.dram_tensor("out_x", OUT_SHAPE, F32, kind="ExternalOutput").ap()
    build(nc, t)
    r = _run(nc, [{f"in_{n}": a for n, a in arrays.items()}], core_ids=[0])
    return r.results[0]["out_x"]
```
